# Optimizing a Trainium2 kernel written in Bass

```python
import numpy as np
import jax
import jax.numpy as jnp

def _softmax(x, axis=-1):
    return jax.nn.softmax(x, axis=axis)

def _gelu(x):
    return jax.nn.gelu(x, approximate=True)

def _silu(x):
    return jax.nn.silu(x)

def _sigmoid(x):
    return jax.nn.sigmoid(x)

def _layernorm(x, axis=-1, eps=1e-05):
    m = jnp.mean(x, axis=axis, keepdims=True)
    v = jnp.var(x, axis=axis, keepdims=True)
    return (x - m) / jnp.sqrt(v + eps)

def _scatter_add(tgt, idx, src, axis=0):
    return tgt.at[idx].add(src)

def _segment_sum(src, seg, n):
    return jax.ops.segment_sum(src, seg, n)
kernel_name = 'mk_gnn_preln_d2_gnn_r8_6f1a69'

def setup_inputs(seed: int=0):
    np.random.seed(seed)
    _w = jnp.asarray

    def _rec_inputs():
        import jax
        import jax.numpy as jnp
        _gk = jax.random.key(seed)
        x = -0.0002117 + 1 * jax.random.normal(jax.random.fold_in(_gk, 1), (1250, 512), jnp.float32)
        src = jax.random.randint(jax.random.fold_in(_gk, 2), (20000,), 0, 1250, jnp.int32)
        dst = jnp.minimum((1250 * jax.random.uniform(jax.random.fold_in(_gk, 3), (20000,)) ** 2.0).astype(jnp.int32), 9999)
        _o = jnp.argsort(dst, stable=True)
        src = src[_o]
        dst = dst[_o]
        edge_attr_64 = 0.000279952 + 1.00013 * jax.random.normal(jax.random.fold_in(_gk, 11), (20000, 64), jnp.float32)
        return (x, src, dst, edge_attr_64)
    x, src, dst, edge_attr_64 = _rec_inputs()

    def _L0_gnn_setup():
        import jax, jax.numpy as jnp
        import numpy as np
        N = 6250
        IN_CH = 512
        OUT_CH = 512
        DEG = 32
        E = N * DEG
        key = jax.random.key(seed)
        kx, kwc, kwn, kb, ke = jax.random.split(key, 5)
        x = jax.random.normal(kx, (N, IN_CH), dtype=jnp.float32)
        bound = 1.0 / np.sqrt(IN_CH)
        wc = jax.random.uniform(kwc, (IN_CH, OUT_CH), minval=-bound, maxval=bound, dtype=jnp.float32)
        wn = jax.random.uniform(kwn, (IN_CH, OUT_CH), minval=-bound, maxval=bound, dtype=jnp.float32)
        bias = jax.random.uniform(kb, (OUT_CH,), minval=-bound, maxval=bound, dtype=jnp.float32)
        src = jnp.repeat(jnp.arange(N, dtype=jnp.int64), DEG)
        dst = jax.random.randint(ke, (E,), 0, N, dtype=jnp.int64)
        edge_index = jnp.stack([src, dst], axis=0)
        return {'x': x, 'wc': wc, 'wn': wn, 'bias': bias, 'edge_index': edge_index}
    _L0_gnn_all = _L0_gnn_setup()
    _L0_gnn_in = {k: v for k, v in _L0_gnn_all.items() if k in ('wc', 'wn', 'bias')}
    del _L0_gnn_all

    def _L1_gnn_setup():
        import jax, jax.numpy as jnp
        import numpy as np
        N_NODES = 2500
        N_EDGES = 40000
        HIDDEN = 512
        EDGE_DIM = 64
        LN_EPS = 1e-05

        def mish(x):
            return x * jnp.tanh(jax.nn.softplus(x))
        key = jax.random.key(seed)
        ks = jax.random.split(key, 8)
        s = lambda fan_in: 1.0 / np.sqrt(fan_in)
        return {'x': jax.random.normal(ks[0], (N_NODES, HIDDEN), dtype=jnp.float32), 'edge_index': jax.random.randint(ks[1], (2, N_EDGES), 0, N_NODES, dtype=jnp.int64), 'edge_attr': jax.random.normal(ks[2], (N_EDGES, EDGE_DIM), dtype=jnp.float32), 'W1': jax.random.normal(ks[3], (2 * HIDDEN + EDGE_DIM, HIDDEN), dtype=jnp.float32) * s(2 * HIDDEN + EDGE_DIM), 'b1': jnp.zeros((HIDDEN,), dtype=jnp.float32), 'W2': jax.random.normal(ks[4], (HIDDEN, HIDDEN), dtype=jnp.float32) * s(HIDDEN), 'b2': jnp.zeros((HIDDEN,), dtype=jnp.float32), 'W3': jax.random.normal(ks[5], (2 * HIDDEN, HIDDEN), dtype=jnp.float32) * s(2 * HIDDEN), 'b3': jnp.zeros((HIDDEN,), dtype=jnp.float32), 'W4': jax.random.normal(ks[6], (HIDDEN, HIDDEN), dtype=jnp.float32) * s(HIDDEN), 'b4': jnp.zeros((HIDDEN,), dtype=jnp.float32), 'gamma': jnp.ones((HIDDEN,), dtype=jnp.float32), 'beta': jnp.zeros((HIDDEN,), dtype=jnp.float32)}
    _L1_gnn_all = _L1_gnn_setup()
    _L1_gnn_in = {k: v for k, v in _L1_gnn_all.items() if k in ('W1', 'b1', 'W2', 'b2', 'W3', 'b3', 'W4', 'b4', 'gamma', 'beta')}
    del _L1_gnn_all
    return {'x': x, 'src': src, 'dst': dst, 'edge_attr_64': edge_attr_64, 'L0_gnn_wc': _L0_gnn_in['wc'], 'L0_gnn_wn': _L0_gnn_in['wn'], 'L0_gnn_bias': _L0_gnn_in['bias'], 'L1_gnn_W1': _L1_gnn_in['W1'], 'L1_gnn_b1': _L1_gnn_in['b1'], 'L1_gnn_W2': _L1_gnn_in['W2'], 'L1_gnn_b2': _L1_gnn_in['b2'], 'L1_gnn_W3': _L1_gnn_in['W3'], 'L1_gnn_b3': _L1_gnn_in['b3'], 'L1_gnn_W4': _L1_gnn_in['W4'], 'L1_gnn_b4': _L1_gnn_in['b4'], 'L1_gnn_gamma': _L1_gnn_in['gamma'], 'L1_gnn_beta': _L1_gnn_in['beta']}

def reference(x, src, dst, edge_attr_64, L0_gnn_wc, L0_gnn_wn, L0_gnn_bias, L1_gnn_W1, L1_gnn_b1, L1_gnn_W2, L1_gnn_b2, L1_gnn_W3, L1_gnn_b3, L1_gnn_W4, L1_gnn_b4, L1_gnn_gamma, L1_gnn_beta):
    import jax
    import jax.numpy as jnp

    def _L0_gnn_ref(x, wc, wn, bias, edge_index):
        import jax, jax.numpy as jnp
        import numpy as np
        N = 6250
        IN_CH = 512
        OUT_CH = 512
        DEG = 32
        E = N * DEG
        alpha = x @ wc
        beta = x @ wn
        src, dst = (edge_index[0], edge_index[1])
        sums = jax.ops.segment_sum(beta[dst], src, num_segments=x.shape[0])
        counts = jax.ops.segment_sum(jnp.ones_like(src, dtype=beta.dtype), src, num_segments=x.shape[0])
        gamma = sums / counts[:, None]
        return alpha + gamma + bias

    def _L1_gnn_ref(x, edge_index, edge_attr, W1, b1, W2, b2, W3, b3, W4, b4, gamma, beta):
        import jax, jax.numpy as jnp
        import numpy as np
        N_NODES = 2500
        N_EDGES = 40000
        HIDDEN = 512
        EDGE_DIM = 64
        LN_EPS = 1e-05

        def mish(x):
            return x * jnp.tanh(jax.nn.softplus(x))
        src, dst = (edge_index[0], edge_index[1])
        edge_feat = jnp.concatenate([x[src], x[dst], edge_attr], axis=-1)
        h = mish(edge_feat @ W1 + b1)
        messages = mish(h @ W2 + b2)
        agg = jax.ops.segment_sum(messages, dst, num_segments=x.shape[0])
        u = mish(jnp.concatenate([x, agg], axis=-1) @ W3 + b3)
        out = u @ W4 + b4
        y = x + out
        mu = jnp.mean(y, axis=-1, keepdims=True)
        var = jnp.mean(jnp.square(y - mu), axis=-1, keepdims=True)
        return (y - mu) * jax.lax.rsqrt(var + LN_EPS) * gamma + beta
    edge_index = jnp.stack([src, dst])
    h = jnp.maximum(_layernorm(x, axis=-1), 0.0)
    x = x + _L0_gnn_ref(h, L0_gnn_wc, L0_gnn_wn, L0_gnn_bias, edge_index)
    h = jnp.maximum(_layernorm(x, axis=-1), 0.0)
    x = x + _L1_gnn_ref(h, edge_index, edge_attr_64, L1_gnn_W1, L1_gnn_b1, L1_gnn_W2, L1_gnn_b2, L1_gnn_W3, L1_gnn_b3, L1_gnn_W4, L1_gnn_b4, L1_gnn_gamma, L1_gnn_beta)
    return x

_drawn_inputs = setup_inputs


def setup_inputs(seed=0):
    import zlib

    import numpy as np

    out = dict(_drawn_inputs(seed))
    spreads = {'L1_gnn_b1': (0.0, 0.1),
     'L1_gnn_b2': (0.0, 0.1),
     'L1_gnn_b3': (0.0, 0.271),
     'L1_gnn_b4': (0.0, 0.1),
     'L1_gnn_gamma': (1.0, 0.2),
     'L1_gnn_beta': (0.0, 0.1)}
    factors = {}
    for name, (base, spread) in spreads.items():
        noise = np.random.default_rng([zlib.crc32(name.encode()), seed]).standard_normal(out[name].shape)
        drawn = base * np.exp(spread * noise) if base else spread * noise
        out[name] = jnp.asarray(drawn.astype(out[name].dtype))
    for name, factor in factors.items():
        out[name] = (out[name] * factor).astype(out[name].dtype)
    return out
```

```python
import concourse.bass as bass
from concourse import mybir
from contextlib import ExitStack

F32 = mybir.dt.float32
F32R = mybir.dt.float32r
BF16 = mybir.dt.bfloat16
F16 = mybir.dt.float16
I32 = mybir.dt.int32
ALU = mybir.AluOpType
ACT = mybir.ActivationFunctionType
AX = mybir.AxisListType

P = 128
NODES = 1250
NT = -(-NODES // P)
NP = NT * P
PAD_NODE = NP - 1
H = 512
KT = H // P
ED = 64
EDGES = 20000
SUPER = 512
SUBS = SUPER // P
NS = -(-EDGES // SUPER)
NSUB = NS * SUBS
LN_EPS = 1e-5
T_MAX = 2.0 ** 31
X_MAX = 20.0
BANK = 512


def row(buffer, t):
    return buffer[:, bass.ds(t, 1), :].rearrange("p a n -> p (a n)")


class Net:
    pass


def prepare_stage(nc, ctx, g, stage):
    sb = lambda name, shape, dt=F32: stage.enter_context(nc.sbuf_tensor("prep_" + name, shape, dt))
    pb = lambda name, shape: stage.enter_context(nc.psum_tensor("prep_" + name, shape, F32))
    sem = lambda name: stage.enter_context(nc.semaphore("prep_" + name))

    wc = sb("wc", [P, KT, H])
    wn = sb("wn", [P, KT, H])
    bias = sb("bias", [P, H])
    stats = sb("stats", [P, NT, 6])
    mv = sb("mv", [P, NT, 2])
    rstd = sb("rstd", [P, NT])
    shift = sb("shift", [P, NT])
    h = [sb(f"h{i}", [P, H]) for i in range(2)]
    hT = [sb(f"hT{i}", [P, KT, P]) for i in range(2)]
    rows_i = sb("rows_i", [NS, SUPER], I32)
    ends = sb("ends", [NS, 2])
    ends_i = sb("ends_i", [NS, 2], I32)
    lohi = sb("lohi", [NS, 2])
    diag = sb("diag", [NS, 2, NS])
    later = sb("later", [NS, P])
    below = sb("below", [NT, NT])
    ones = sb("ones", [NS, P])
    tile_id = sb("tile_id", [P, 1])
    chunk = sb("chunk", [P, NS])
    over = sb("over", [P, 4, NS])
    span = sb("span", [NT, 4])
    span_i = sb("span_i", [NT, 4], I32)
    wins = sb("wins", [NS, 4])
    wins_i = sb("wins_i", [NS, 4], I32)
    zero4 = sb("zero4", [1, 4], I32)
    p_T = [pb(f"p_T{i}", [P, KT * P]) for i in range(2)]
    p_a = [pb(f"p_a{i}", [P, H]) for i in range(2)]
    p_b = [pb(f"p_b{i}", [P, H]) for i in range(2)]
    p_lh = pb("p_lh", [P, 2 * NS])
    p_base = pb("p_base", [P, 4])

    x_in, w_in, i_in = sem("x_in"), sem("w_in"), sem("i_in")
    const_ready = sem("const_ready")
    stat_step = sem("stat_step")
    ln_step = sem("ln_step")
    shift_ready = sem("shift_ready")
    h_ready, hT_psum, hT_ready = sem("h_ready"), sem("hT_psum"), sem("hT_ready")
    alpha_psum, beta_psum = sem("alpha_psum"), sem("beta_psum")
    alpha_done, beta_done = sem("alpha_done"), sem("beta_done")
    xb_done = sem("xb_done")
    tab = sem("tab")
    tab_pe = sem("tab_pe")
    tab_out = sem("tab_out")

    with nc.Block() as block:

        @block.sync
        def _(sp):
            sp.dma_start(g.x1[:, :, :], g.x.rearrange("(t p) f -> p t f", p=P)).then_inc(x_in, 16)
            sp.dma_start(rows_i[:, :], g.dst_rows).then_inc(i_in, 16)
            sp.dma_start(g.src_i[:, :], g.src_cols).then_inc(i_in, 16)
            sp.dma_start(g.dst_i[:, :], g.dst_cols).then_inc(i_in, 16)
            sp.dma_start(bias[:, :], g.bias.rearrange("(a n) -> a n", a=1).to_broadcast([P, H])).then_inc(w_in, 16)
            sp.dma_start(wc[:, :, :], g.wc.rearrange("(k p) n -> p k n", p=P)).then_inc(w_in, 16)
            sp.dma_start(wn[:, :, :], g.wn.rearrange("(k p) n -> p k n", p=P)).then_inc(w_in, 16)
            sp.wait_ge(tab, TAB_DONE)
            sp.dma_start(g.spans, span_i[:, :]).then_inc(tab_out, 16)
            sp.dma_start(g.wins[0:NS, 0:1], wins_i[:, 0:1], allow_slow_non_contiguous=True).then_inc(tab_out, 16)
            sp.dma_start(g.wins[1:NS + 1, 1:4], wins_i[:, 1:4]).then_inc(tab_out, 16)
            sp.dma_start(g.wins[0:1, 1:4], zero4[:, 1:4]).then_inc(tab_out, 16)
            sp.dma_start(g.wins[NS:NS + 1, 0:1], zero4[:, 0:1]).then_inc(tab_out, 16)
            sp.wait_ge(tab_out, 80)

        @block.gpsimd
        def _(pool):
            pool.memset(g.ident[:, :], 0.0).then_inc(const_ready, 1)
            pool.wait_ge(const_ready, 1)
            pool.affine_select(out=g.ident[:, :], in_=g.ident[:, :], compare_op=ALU.not_equal, fill=1.0,
                               base=0, pattern=[[-1, P]], channel_multiplier=1).then_inc(const_ready, 1)
            pool.memset(later[:, :], 0.0).then_inc(const_ready, 1)
            pool.wait_ge(const_ready, 3)
            pool.affine_select(out=later[:, :], in_=later[:, :], compare_op=ALU.is_ge, fill=1.0,
                               base=0, pattern=[[-1, P]], channel_multiplier=1).then_inc(const_ready, 1)
            pool.memset(ones[:, :], 1.0).then_inc(const_ready, 1)
            pool.iota(g.iota[:, :], pattern=[[1, NP]], base=0, channel_multiplier=0,
                      allow_small_or_imprecise_dtypes=True).then_inc(const_ready, 1)
            pool.iota(tile_id[:, :], pattern=[[0, 1]], base=0, channel_multiplier=1,
                      allow_small_or_imprecise_dtypes=True).then_inc(const_ready, 1)
            pool.iota(chunk[:, :], pattern=[[1, NS]], base=0, channel_multiplier=0,
                      allow_small_or_imprecise_dtypes=True).then_inc(const_ready, 1)
            pool.memset(zero4[:, :], 0).then_inc(const_ready, 1)
            pool.memset(g.eps[:, :], LN_EPS).then_inc(const_ready, 1)

        CONST = 10

        @block.vector
        def _(dve):
            n = 0
            dve.wait_ge(i_in, 48)
            dve.wait_ge(const_ready, CONST)

            def step(ins):
                nonlocal n
                n += 1
                ins.then_inc(tab, 1)

            step(dve.tensor_reduce(ends[:, 0:1], rows_i[:, :], AX.X, ALU.min))
            step(dve.tensor_reduce(ends[:, 1:2], rows_i[:, :], AX.X, ALU.max))
            step(dve.tensor_copy(g.srcf[:, :], g.src_i[:, :]))
            step(dve.tensor_copy(g.dstf[:, :], g.dst_i[:, :]))
            step(dve.tensor_copy(g.iota16[:, :], g.iota[:, :]))
            dve.wait_ge(tab, 2)
            step(dve.tensor_copy(ends_i[:, :], ends[:, :]))
            dve.wait_ge(tab, n)
            step(dve.tensor_scalar(ends_i[:, :], ends_i[:, :], 7, None, ALU.arith_shift_right))
            dve.wait_ge(tab, n)
            step(dve.tensor_copy(lohi[:, :], ends_i[:, :]))
            dve.wait_ge(tab, n)
            step(dve.tensor_copy(wins[:, 0:1], lohi[:, 0:1]))
            step(dve.tensor_copy(wins[:, 1:2], lohi[:, 0:1]))
            step(dve.tensor_sub(wins[:, 2:3], lohi[:, 1:2], lohi[:, 0:1]))
            step(dve.tensor_scalar(diag[:, 0, :], g.ident[0:NS, 0:NS], lohi[:, 0:1], None, ALU.mult))
            step(dve.tensor_scalar(diag[:, 1, :], g.ident[0:NS, 0:NS], lohi[:, 1:2], None, ALU.mult))
            dve.wait_ge(tab_pe, 1)
            step(dve.tensor_scalar(over[:, 0, :], p_lh[:, 0:NS], tile_id[:, 0:1], None, ALU.is_le))
            step(dve.tensor_scalar(over[:, 1, :], p_lh[:, NS:2 * NS], tile_id[:, 0:1], None, ALU.is_ge))
            dve.wait_ge(tab, n)
            step(dve.tensor_tensor(over[:, 2, :], over[:, 0, :], over[:, 1, :], ALU.mult))
            dve.wait_ge(tab, n)
            step(dve.tensor_tensor(over[:, 0, :], over[:, 2, :], chunk[:, :], ALU.mult))
            step(dve.scalar_tensor_tensor(out=over[:, 3, :], in0=over[:, 2, :], scalar=-float(NS),
                                          in1=chunk[:, :], op0=ALU.mult, op1=ALU.add))
            dve.wait_ge(tab, n)
            step(dve.tensor_reduce(span[:, 1:2], over[0:NT, 0, :], AX.X, ALU.max))
            step(dve.tensor_reduce(span[:, 3:4], over[0:NT, 3, :], AX.X, ALU.min))
            dve.wait_ge(tab, n)
            step(dve.tensor_scalar(span[:, 3:4], span[:, 3:4], float(NS), None, ALU.add))
            dve.wait_ge(tab, n)
            step(dve.tensor_tensor(span[:, 0:1], span[:, 3:4], span[:, 1:2], ALU.min))
            dve.wait_ge(tab, n)
            step(dve.tensor_sub(span[:, 3:4], span[:, 1:2], span[:, 0:1]))
            dve.wait_ge(tab, n)
            step(dve.tensor_scalar(span[:, 1:2], span[:, 3:4], 1.0, None, ALU.add))
            assert n == TAB_SPAN
            dve.wait_ge(tab_pe, 2)
            step(dve.tensor_copy(span[:, 2:3], p_base[0:NT, 0:1]))
            step(dve.tensor_copy(wins[:, 3:4], p_base[0:NS, 1:2]))
            dve.wait_ge(tab, n)
            step(dve.tensor_copy(span_i[:, :], span[:, :]))
            step(dve.tensor_copy(wins_i[:, :], wins[:, :]))
            assert n == TAB_DONE

            dve.wait_ge(x_in, 16)
            for t in range(NT):
                dve.bn_stats(stats[:, t, :], g.x1[:, t, :]).then_inc(stat_step, 1)
            for t in range(NT):
                dve.wait_ge(stat_step, t + 1)
                dve.bn_aggr(mv[:, t, :], stats[:, t, :]).then_inc(stat_step, 1)
            dve.wait_ge(ln_step, 2)
            dve.scalar_tensor_tensor(out=shift[:, :], in0=mv[:, :, 0], scalar=-1.0, in1=rstd[:, :],
                                     op0=ALU.mult, op1=ALU.mult).then_inc(shift_ready, 1)
            dve.wait_ge(w_in, 48)

            def transposed(t, u):
                dve.wait_ge(hT_psum, t + 1)
                if isinstance(t, int) and t < 2:
                    pass
                else:
                    dve.wait_ge(beta_psum, t - 1)
                dve.tensor_copy(hT[u][:, :, :], p_T[u][:, :].rearrange("p (k m) -> p k m", k=KT)) \
                   .then_inc(hT_ready, 1)

            def alpha(t, u):
                dve.wait_ge(h_ready, t + 1)
                dve.tensor_tensor(row(g.x1, t), row(g.x1, t), bias[:, :], ALU.add).then_inc(xb_done, 1)
                dve.wait_ge(alpha_psum, t + 1)
                dve.wait_ge(xb_done, t + 1)
                dve.tensor_tensor(row(g.x1, t), row(g.x1, t), p_a[u][:, :], ALU.add).then_inc(alpha_done, 1)

            transposed(0, 0)
            transposed(1, 1)
            alpha(0, 0)
            with dve.Fori(1, NT // 2) as pair:
                for u in range(2):
                    transposed(2 * pair + u, u)
                    alpha(2 * pair + u - 1, 1 - u)
            alpha(NT - 1, 1)

        @block.scalar
        def _(act):
            act.preload_act_table_set("natural_log_exp_and_others")
            act.wait_ge(stat_step, 2 * NT)
            act.activation(rstd[:, :], mv[:, :, 1], ACT.Ln, bias=g.eps[:, 0:1]).then_inc(ln_step, 1)
            act.wait_ge(ln_step, 1)
            act.activation(rstd[:, :], rstd[:, :], ACT.Exp, scale=-0.5).then_inc(ln_step, 1)
            act.wait_ge(shift_ready, 1)

            def normalise(t, u):
                if not isinstance(t, int) or t >= 2:
                    act.wait_ge(hT_psum, t - 1)
                act.activation(h[u][:, :], row(g.x1, t), ACT.Relu, bias=shift[:, bass.ds(t, 1)],
                               scale=rstd[:, bass.ds(t, 1)]).then_inc(h_ready, 1)

            def beta(t, u):
                act.wait_ge(beta_psum, t + 1)
                act.activation(row(g.beta, t), p_b[u][:, :], ACT.Copy).then_inc(beta_done, 1)

            normalise(0, 0)
            normalise(1, 1)
            beta(0, 0)
            with act.Fori(1, NT // 2) as pair:
                for u in range(2):
                    normalise(2 * pair + u, u)
                    beta(2 * pair + u - 1, 1 - u)
            beta(NT - 1, 1)

        @block.tensor
        def _(pe):
            pe.wait_ge(const_ready, CONST)
            pe.wait_ge(tab, TAB_DIAG)
            nc.tensor.matmul(p_lh[:, :], ones[:, :], diag[:, :, :].rearrange("k a c -> k (a c)"),
                             start=True, stop=True).then_inc(tab_pe, 1)
            pe.wait_ge(tab, TAB_SPAN)
            nc.tensor.matmul(p_base[:, 0:1], later[0:NT, :], span[:, 1:2], start=True, stop=True)
            nc.tensor.matmul(p_base[:, 1:2], later[:, :], wins[:, 2:3], start=True, stop=True).then_inc(tab_pe, 1)

            def transposes(t, u):
                pe.wait_ge(h_ready, t + 1)
                if not isinstance(t, int) or t >= 2:
                    pe.wait_ge(hT_ready, t - 1)
                for k in range(KT):
                    last = nc.tensor.transpose(p_T[u][:, k * P:(k + 1) * P], h[u][:, k * P:(k + 1) * P], g.ident[:, :])
                last.then_inc(hT_psum, 1)

            def products(t, u):
                pe.wait_ge(hT_ready, t + 1)
                if not isinstance(t, int) or t >= 2:
                    pe.wait_ge(alpha_done, t - 1)
                    pe.wait_ge(beta_done, t - 1)
                for out, w, signal in ((p_a[u], wc, alpha_psum), (p_b[u], wn, beta_psum)):
                    for k in range(KT):
                        last = nc.tensor.matmul(out[:, :], hT[u][:, k, :], w[:, k, :], start=k == 0, stop=k == KT - 1)
                    last.then_inc(signal, 1)

            transposes(0, 0)
            transposes(1, 1)
            pe.wait_ge(w_in, 48)
            products(0, 0)
            with pe.Fori(1, NT // 2) as pair:
                for u in range(2):
                    transposes(2 * pair + u, u)
                    products(2 * pair + u - 1, 1 - u)
            products(NT - 1, 1)


TAB_DIAG, TAB_SPAN, TAB_DONE = 13, 24, 28


def adjacency_stage(nc, ctx, g, stage):
    sb = lambda name, shape, dt=F32: stage.enter_context(nc.sbuf_tensor("adj_" + name, shape, dt))
    pb = lambda name, shape: stage.enter_context(nc.psum_tensor("adj_" + name, shape, F32))
    sem = lambda name: stage.enter_context(nc.semaphore("adj_" + name))

    oh_src = [sb(f"oh_src{j}", [P, NP], BF16) for j in range(SUBS)]
    oh_dst = [sb(f"oh_dst{j}", [P, P], BF16) for j in range(SUBS)]
    zeros = sb("zeros", [P, BANK], BF16)
    p_adj = [pb(f"p_adj{u}", [P, 3 * BANK]) for u in range(2)]
    zero_ready = sem("zero_ready")
    hot_src = sem("hot_src")
    hot_dst = sem("hot_dst")
    slot_free = sem("slot_free")
    adj_psum = sem("adj_psum")
    adj_done = sem("adj_done")
    COLS = [(c, min(BANK, NP - c)) for c in range(0, NP, BANK)]

    def span_of(eng, t):
        _, (first, count, before) = nc.values_load_multi_w_load_instructions(
            g.spans[bass.ds(t, 1), 0:3], engines=[eng.engine], min_val=0, max_val=NS * NT)
        return nc.s_assert_le(first, NS - 1), nc.s_assert_le(count, NS), before

    with nc.Block() as block:

        @block.gpsimd
        def _(pool):
            pool.memset(zeros[:, :], 0.0).then_inc(zero_ready, 1)
            pool.nop().then_inc(slot_free, SUBS)

        @block.vector
        def _(dve):
            with dve.Fori(0, NT) as t:
                first, count, before = span_of(dve, t)
                with dve.Fori(0, count) as k:
                    c = nc.s_assert_le(first + k, NS - 1)
                    for j in range(SUBS):
                        n = (before + k) * SUBS + j
                        dve.wait_ge(slot_free, n + 1)
                        dve.tensor_scalar(oh_src[j][:, :], g.iota16[:, :], g.srcf[:, bass.ds(c * SUBS + j, 1)],
                                          None, ALU.is_equal).then_inc(hot_src, 1)
                        dve.tensor_scalar(oh_dst[j][:, :], g.iota16[:, bass.ds(t * P, P)],
                                          g.dstf[:, bass.ds(c * SUBS + j, 1)], None, ALU.is_equal).then_inc(hot_dst, 1)

        @block.tensor
        def _(pe):
            pe.wait_ge(zero_ready, 1)

            def tile(t, u, first_use):
                first, count, before = span_of(pe, t)
                if not first_use:
                    pe.wait_ge(adj_done, t - 1)
                for c0, w in COLS:
                    nc.tensor.matmul(p_adj[u][:, c0:c0 + w], zeros[:, 0:P], zeros[:, 0:w], start=True, stop=False)
                with pe.Fori(0, count) as k:
                    for j in range(SUBS):
                        n = (before + k) * SUBS + j
                        pe.wait_ge(hot_dst, n + 1)
                        for c0, w in COLS:
                            last = nc.tensor.matmul(p_adj[u][:, c0:c0 + w], oh_dst[j][:, :], oh_src[j][:, c0:c0 + w],
                                                    start=False, stop=False)
                        last.then_inc(slot_free, 1)
                for c0, w in COLS:
                    last = nc.tensor.matmul(p_adj[u][:, c0:c0 + w], zeros[:, 0:P], zeros[:, 0:w], start=False, stop=True)
                last.then_inc(adj_psum, 1)

            tile(0, 0, True)
            tile(1, 1, True)
            with pe.Fori(1, NT // 2) as pair:
                for u in range(2):
                    tile(2 * pair + u, u, False)

        @block.scalar
        def _(act):
            with act.Fori(0, NT // 2) as pair:
                for u in range(2):
                    act.wait_ge(adj_psum, 2 * pair + u + 1)
                    act.activation(row(g.adj, 2 * pair + u), p_adj[u][:, 0:NP], ACT.Copy).then_inc(adj_done, 1)


def node_stage(nc, ctx, g, stage):
    sb = lambda name, shape, dt=F32: stage.enter_context(nc.sbuf_tensor("node_" + name, shape, dt))
    pb = lambda name, shape: stage.enter_context(nc.psum_tensor("node_" + name, shape, F32))
    sem = lambda name: stage.enter_context(nc.semaphore("node_" + name))

    w = [sb(f"w{i}", [P, KT, H]) for i in range(3)]
    b1, b3 = sb("b1", [P, H]), sb("b3", [P, H])
    ones = sb("ones", [P, 1])
    adjs = [sb(f"adjs{u}", [P, NT, P]) for u in range(2)]
    deg = sb("deg", [P, NT])
    inv = [sb(f"inv{u}", [P, 1]) for u in range(2)]
    stats = [sb(f"stats{u}", [P, 6]) for u in range(2)]
    mv = [sb(f"mv{u}", [P, 2]) for u in range(2)]
    rstd = [sb(f"rstd{u}", [P, 1]) for u in range(2)]
    shift = [sb(f"shift{u}", [P, 1]) for u in range(2)]
    h = [sb(f"h{u}", [P, H]) for u in range(2)]
    hT = [sb(f"hT{u}", [P, KT, P]) for u in range(2)]
    out_s = [sb(f"out_s{u}", [P, H]) for u in range(2)]
    out_d = [sb(f"out_d{u}", [P, H]) for u in range(2)]
    p_sum = [pb(f"p_sum{u}", [P, H]) for u in range(2)]
    p_deg = pb("p_deg", [P, 1])
    p_T = [pb(f"p_T{u}", [P, KT * P]) for u in range(2)]
    p_o = [pb(f"p_o{i}", [P, H]) for i in range(3)]

    w_in = sem("w_in")
    ones_ready = sem("ones_ready")
    waited = sem("waited")
    adjs_ready, sum_psum, deg_psum = sem("adjs_ready"), sem("sum_psum"), sem("deg_psum")
    deg_read, inv_step, x1_ready, stat_step = sem("deg_read"), sem("inv_step"), sem("x1_ready"), sem("stat_step")
    ln_step, shift_ready, h_ready, h_kept = sem("ln_step"), sem("shift_ready"), sem("h_ready"), sem("h_kept")
    hT_psum, hT_ready = sem("hT_psum"), sem("hT_ready")
    o_psum = [sem(f"o_psum{i}") for i in range(3)]
    o_done = [sem(f"o_done{i}") for i in range(3)]
    stored = [sem(f"stored{u}") for u in range(2)]

    def later(t, n):
        return not isinstance(t, int) or t >= n

    with nc.Block() as block:

        @block.sync
        def _(sp):
            for i, part in enumerate((g.w1[0:H, :], g.w1[H:2 * H, :], g.w3[0:H, :])):
                sp.dma_start(w[i][:, :, :], part.rearrange("(k p) n -> p k n", p=P)).then_inc(w_in, 16)
            sp.dma_start(b1[:, :], g.b1.rearrange("(a n) -> a n", a=1).to_broadcast([P, H])).then_inc(w_in, 16)
            sp.dma_start(b3[:, :], g.b3.rearrange("(a n) -> a n", a=1).to_broadcast([P, H])).then_inc(w_in, 16)
            with sp.Fori(0, NT // 2) as pair:
                for u in range(2):
                    t = 2 * pair + u
                    sp.wait_ge(o_done[0], t + 1)
                    sp.dma_start(g.tab_src[bass.ds(t * P, P), :], out_s[u][:, :]).then_inc(stored[u], 16)
                    sp.wait_ge(o_done[1], t + 1)
                    sp.dma_start(g.tab_dst[bass.ds(t * P, P), :], out_d[u][:, :]).then_inc(stored[u], 16)
            for u in range(2):
                sp.wait_ge(stored[u], 32 * (NT // 2))

        @block.gpsimd
        def _(pool):
            pool.memset(ones[:, :], 1.0).then_inc(ones_ready, 1)
            pool.memset(g.nan0[:, :], 0.0).then_inc(ones_ready, 1)

        @block.tensor
        def _(pe):
            pe.wait_ge(ones_ready, 1)

            def sums(t, u):
                pe.wait_ge(adjs_ready, t + 1)
                if later(t, 2):
                    pe.wait_ge(x1_ready, t - 1)
                if later(t, 1):
                    pe.wait_ge(deg_read, t)
                for d in range(NT):
                    last = nc.tensor.matmul(p_sum[u][:, :], adjs[u][:, d, :], g.beta[:, d, :], start=d == 0, stop=d == NT - 1)
                last.then_inc(sum_psum, 1)
                for d in range(NT):
                    last = nc.tensor.matmul(p_deg[:, :], adjs[u][:, d, :], ones[:, :], start=d == 0, stop=d == NT - 1)
                last.then_inc(deg_psum, 1)

            def transposes(t, u):
                pe.wait_ge(h_ready, t + 1)
                if later(t, 2):
                    pe.wait_ge(hT_ready, t - 1)
                for k in range(KT):
                    last = nc.tensor.transpose(p_T[u][:, k * P:(k + 1) * P], h[u][:, k * P:(k + 1) * P], g.ident[:, :])
                last.then_inc(hT_psum, 1)

            def products(t, u):
                pe.wait_ge(hT_ready, t + 1)
                for i in range(3):
                    if later(t, 1):
                        pe.wait_ge(o_done[i], t)
                    for k in range(KT):
                        last = nc.tensor.matmul(p_o[i][:, :], hT[u][:, k, :], w[i][:, k, :], start=k == 0, stop=k == KT - 1)
                    last.then_inc(o_psum[i], 1)

            sums(0, 0)
            pe.wait_ge(w_in, 80)
            sums(1, 1)
            transposes(0, 0)
            products(0, 0)
            with pe.Fori(1, NT // 2) as pair:
                for u in range(2):
                    t = 2 * pair + u
                    sums(t, u)
                    transposes(t - 1, 1 - u)
                    products(t - 1, 1 - u)
            transposes(NT - 1, 1)
            products(NT - 1, 1)

        @block.scalar
        def _(act):
            def stage_adj(t, u):
                if later(t, 2):
                    act.wait_ge(deg_psum, t - 1)
                act.activation(adjs[u][:, :, :], g.adj[:, :, bass.ds(t * P, P)], ACT.Copy).then_inc(adjs_ready, 1)

            def normalise(t, u):
                act.wait_ge(stat_step, 2 * t + 2)
                if later(t, 2):
                    act.wait_ge(h_kept, t - 1)
                act.activation(rstd[u][:, :], mv[u][:, 1:2], ACT.Ln, bias=g.eps[:, 0:1]).then_inc(ln_step, 1)
                act.wait_ge(ln_step, 2 * t + 1)
                act.activation(rstd[u][:, :], rstd[u][:, :], ACT.Exp, scale=-0.5).then_inc(ln_step, 1)
                act.wait_ge(shift_ready, t + 1)
                if later(t, 2):
                    act.wait_ge(hT_psum, t - 1)
                act.activation(h[u][:, :], row(g.x1, t), ACT.Relu, bias=shift[u][:, 0:1],
                               scale=rstd[u][:, 0:1]).then_inc(h_ready, 1)
                act.activation(row(g.h1, t), row(g.x1, t), ACT.Relu, bias=shift[u][:, 0:1],
                               scale=rstd[u][:, 0:1]).then_inc(h_kept, 1)

            def destination(t, u):
                act.wait_ge(o_psum[1], t + 1)
                if later(t, 2):
                    act.wait_ge(stored[u], 16 * (t - u))
                act.activation(out_d[u][:, :], p_o[1][:, :], ACT.Copy).then_inc(o_done[1], 1)

            stage_adj(0, 0)
            stage_adj(1, 1)
            normalise(0, 0)
            for t in range(2):
                stage_adj(t + 2, t)
                normalise(t + 1, 1 - t)
                destination(t, t)
            with act.Fori(1, NT // 2 - 1) as pair:
                for u in range(2):
                    t = 2 * pair + u
                    stage_adj(t + 2, u)
                    normalise(t + 1, 1 - u)
                    destination(t, u)
            normalise(NT - 1, 1)
            destination(NT - 2, 0)
            destination(NT - 1, 1)

        @block.vector
        def _(dve):
            def mean_of_neighbours(t, u):
                one = slice(None), bass.ds(t, 1)
                dve.wait_ge(deg_psum, t + 1)
                dve.tensor_copy(deg[one], p_deg[:, :]).then_inc(deg_read, 1)
                dve.wait_ge(deg_read, t + 1)
                dve.tensor_scalar(inv[u][:, :], deg[one], 1.0, None, ALU.max).then_inc(inv_step, 1)
                dve.wait_ge(inv_step, 2 * t + 1)
                dve.reciprocal(inv[u][:, :], inv[u][:, :]).then_inc(inv_step, 1)
                dve.wait_ge(inv_step, 2 * t + 2)
                dve.scalar_tensor_tensor(out=row(g.x1, t), in0=p_sum[u][:, :], scalar=inv[u][:, 0:1], in1=row(g.x1, t),
                                         op0=ALU.mult, op1=ALU.add).then_inc(x1_ready, 1)
                dve.wait_ge(x1_ready, t + 1)
                dve.sem_inc(waited, 1)
                dve.bn_stats(stats[u][:, :], row(g.x1, t)).then_inc(stat_step, 1)
                dve.wait_ge(stat_step, 2 * t + 1)
                dve.sem_inc(waited, 1)
                dve.bn_aggr(mv[u][:, :], stats[u][:, :]).then_inc(stat_step, 1)
                dve.wait_ge(ln_step, 2 * t + 2)
                dve.scalar_tensor_tensor(out=shift[u][:, :], in0=mv[u][:, 0:1], scalar=-1.0, in1=rstd[u][:, :],
                                         op0=ALU.mult, op1=ALU.mult).then_inc(shift_ready, 1)

            def transposed(t, u):
                dve.wait_ge(hT_psum, t + 1)
                if later(t, 2):
                    dve.wait_ge(o_psum[2], t - 1)
                dve.tensor_copy(hT[u][:, :, :], p_T[u][:, :].rearrange("p (k m) -> p k m", k=KT)).then_inc(hT_ready, 1)

            def source_and_own(t, u):
                dve.wait_ge(o_psum[0], t + 1)
                if later(t, 2):
                    dve.wait_ge(stored[u], 16 * (t - u))
                dve.tensor_tensor(out_s[u][:, :], p_o[0][:, :], b1[:, :], ALU.add).then_inc(o_done[0], 1)
                dve.wait_ge(o_psum[2], t + 1)
                dve.tensor_tensor(row(g.own, t), p_o[2][:, :], b3[:, :], ALU.add).then_inc(o_done[2], 1)

            mean_of_neighbours(0, 0)
            dve.wait_ge(w_in, 80)
            for t in range(2):
                transposed(t, t)
                mean_of_neighbours(t + 1, 1 - t)
                source_and_own(t, t)
            with dve.Fori(1, NT // 2 - 1) as pair:
                for u in range(2):
                    t = 2 * pair + u
                    transposed(t, u)
                    mean_of_neighbours(t + 1, 1 - u)
                    source_and_own(t, u)
            transposed(NT - 2, 0)
            mean_of_neighbours(NT - 1, 1)
            source_and_own(NT - 2, 0)
            transposed(NT - 1, 1)
            source_and_own(NT - 1, 1)
            dve.wait_ge(ones_ready, 2)
            for rows, tiles in ((P, slice(0, NT - 1)), (NODES - (NT - 1) * P, slice(NT - 1, NT))):
                dve.reciprocal(g.nan0[0:rows, tiles], deg[0:rows, tiles]).then_inc(inv_step, 1)
            dve.wait_ge(inv_step, 2 * NT + 2)
            for rows, tiles in ((P, slice(0, NT - 1)), (NODES - (NT - 1) * P, slice(NT - 1, NT))):
                dve.tensor_scalar(g.nan0[0:rows, tiles], g.nan0[0:rows, tiles], 0.0, None, ALU.mult).then_inc(inv_step, 1)


def edge_stage(nc, ctx, g, stage):
    sb = lambda name, shape, dt=F32: stage.enter_context(nc.sbuf_tensor("edge_" + name, shape, dt))
    pb = lambda name, shape: stage.enter_context(nc.psum_tensor("edge_" + name, shape, F32))
    sem = lambda name: stage.enter_context(nc.semaphore("edge_" + name))

    HALF = SUPER // 2
    w1f = sb("w1f", [P, H])
    w1_hi, w1_lo = sb("w1_hi", [P, H], F32R), sb("w1_lo", [P, H], F32R)
    w2f = sb("w2f", [P, KT, H])
    w2_hi, w2_lo = sb("w2_hi", [P, KT, H], F32R), sb("w2_lo", [P, KT, H], F32R)
    b2f = sb("b2f", [33, H])
    b2_parts = sb("b2_parts", [P, H], F32R)
    ones = sb("ones", [P, P], F32R)
    onesf = sb("onesf", [P, P])
    idx_s, idx_d = sb("idx_s", [P, SUBS], I32), sb("idx_d", [P, SUBS], I32)
    rows = [sb(f"rows{q}", [P, H]) for q in range(SUBS)]
    attr = [sb(f"attr{b}", [P, HALF]) for b in range(2)]
    attr_parts = [sb(f"attr_parts{b}", [P, HALF], F32R) for b in range(2)]
    th = [[sb(f"th{b}{i}", [P, BANK]) for i in range(2)] for b in range(2)]
    h_hi = [sb(f"h_hi{b}", [P, KT, HALF], F32R) for b in range(2)]
    h_lo = [sb(f"h_lo{b}", [P, KT, HALF], F32R) for b in range(2)]
    tz = [sb(f"tz{i}", [P, BANK]) for i in range(2)]
    msg = [sb(f"msg{b}", [P, 2, H]) for b in range(2)]
    hot = sb("hot", [P, SUBS, P])
    hot_x = sb("hot_x", [P, SUBS, P])

    p_pre = [[pb(f"p_pre{b}{i}", [P, BANK]) for i in range(2)] for b in range(2)]
    p_z = [pb(f"p_z{i}", [P, BANK]) for i in range(2)]
    p_seg = pb("p_seg", [P, H])
    p_x = pb("p_x", [P, H])

    w_in = sem("w_in")
    const_ready = sem("const_ready")
    w_ready = sem("w_ready")
    waited = sem("waited")
    idx_ready = sem("idx_ready")
    src_in = [sem(f"src_in{q}") for q in range(SUBS)]
    dst_in = [sem(f"dst_in{q}") for q in range(SUBS)]
    attr_in = [sem(f"attr_in{b}") for b in range(2)]
    attr_hi, attr_ready = sem("attr_hi"), sem("attr_ready")
    pre_psum = sem("pre_psum")
    h_exp, h_min, h_u, h_ln, h_inv, h_done, h_hi_ready, h_lo_ready = (
        sem(n) for n in ("h_exp", "h_min", "h_u", "h_ln", "h_inv", "h_done", "h_hi_ready", "h_lo_ready"))
    z_psum = sem("z_psum")
    z_exp, z_min, z_u, z_ln, z_inv, m_done = (sem(n) for n in ("z_exp", "z_min", "z_u", "z_ln", "z_inv", "m_done"))
    hot_ready, seg_half, agg_done = sem("hot_ready"), sem("seg_half"), sem("agg_done")
    hot_x_ready, x_psum = sem("hot_x_ready"), sem("x_psum")
    x_added = sem("x_added")

    def after(s, b):
        return (s, 1) if b == 0 else (s + 1, 0)

    def before(s, b):
        return (s - 1, 1) if b == 0 else (s, 0)

    def exists(s):
        return not isinstance(s, int) or 0 <= s < NS

    def steps(eng, step, prologue, epilogue):
        prologue()
        for b in range(2):
            step(0, b)
        with eng.Fori(1, NS - 1) as s:
            for b in range(2):
                step(s, b)
        for b in range(2):
            step(NS - 1, b)
        epilogue()

    def window(eng, s, both=True):
        k = 0 if both else 2
        _, values = nc.values_load_multi_w_load_instructions(g.wins[bass.ds(s, 1), k:4], engines=[eng.engine],
                                                             min_val=0, max_val=NS * NT)
        bound = lambda v: nc.s_assert_le(v, NT - 1)
        return [bound(v) for v in values[:-1]] + [values[-1]]

    with nc.Block() as block:

        @block.sync
        def _(sp):
            sp.dma_start(w1f[0:ED, :], g.w1[2 * H:2 * H + ED, :]).then_inc(w_in, 16)
            sp.dma_start(w1f[ED:2 * ED, :], g.w1[2 * H:2 * H + ED, :]).then_inc(w_in, 16)
            sp.dma_start(b2f[0:1, :], g.b2.rearrange("(a n) -> a n", a=1)).then_inc(w_in, 16)
            sp.dma_start(b2f[32:33, :], g.b2.rearrange("(a n) -> a n", a=1)).then_inc(w_in, 16)
            sp.dma_start(w2f[:, :, :], g.w2.rearrange("(k p) n -> p k n", p=P)).then_inc(w_in, 16)

            def load(s, b):
                if not isinstance(s, int) or s >= 1:
                    sp.wait_ge(attr_ready, 2 * (s - 1) + b + 1)
                part = g.attr_t[:, bass.ds(s * SUPER + b * HALF, HALF)]
                sp.dma_start(attr[b][0:ED, :], part).then_inc(attr_in[b], 16)
                sp.dma_start(attr[b][ED:2 * ED, :], part).then_inc(attr_in[b], 16)

            for b in range(2):
                load(0, b)
            with sp.Fori(1, NS) as s:
                for b in range(2):
                    load(s, b)

        @block.gpsimd
        def _(pool):
            pool.memset(b2_parts[:, :].bitcast(F32), 0.0).then_inc(const_ready, 1)
            pool.memset(onesf[:, :], 1.0).then_inc(const_ready, 1)
            pool.memset(g.agg[:, :, :], 0.0).then_inc(const_ready, 1)
            pool.nop().then_inc(x_added, 1)

            def gather(s, q):
                if not isinstance(s, int) or s >= 1:
                    pool.wait_ge(pre_psum, 4 * (s - 1) + 2 * (q // 2) + 2)
                    pool.sem_inc(waited, 1)
                pool.indirect_dma_start(out=rows[q][:, :], out_offset=None, in_=g.tab_src,
                                        in_offset=bass.IndirectOffsetOnAxis(ap=idx_s[:, q:q + 1], axis=0)).then_inc(src_in[q], 16)

            def gather_add(s, q):
                pool.wait_ge(src_in[q], 16 * (s + 1))
                pool.sem_inc(waited, 1)
                pool.indirect_dma_start(out=rows[q][:, :], out_offset=None, in_=g.tab_dst,
                                        in_offset=bass.IndirectOffsetOnAxis(ap=idx_d[:, q:q + 1], axis=0),
                                        compute_op=ALU.add).then_inc(dst_in[q], 16)

            def superchunk(s):
                if not isinstance(s, int) or s >= 1:
                    for q in range(SUBS):
                        pool.wait_ge(dst_in[q], 16 * s)
                pool.tensor_copy(idx_s[:, :], g.src_i[:, bass.ds(s * SUBS, SUBS)]).then_inc(idx_ready, 1)
                pool.tensor_copy(idx_d[:, :], g.dst_i[:, bass.ds(s * SUBS, SUBS)]).then_inc(idx_ready, 1)
                pool.wait_ge(idx_ready, 2 * s + 2)
                for b in range(2):
                    for q in (2 * b, 2 * b + 1):
                        gather(s, q)
                    for q in (2 * b, 2 * b + 1):
                        gather_add(s, q)

            superchunk(0)
            with pool.Fori(1, NS) as s:
                superchunk(s)

        @block.tensor
        def _(pe):
            def pre(s, b):
                pe.wait_ge(attr_ready, 2 * s + b + 1)
                for i in range(2):
                    if not isinstance(s, int) or s >= 1:
                        pe.wait_ge(h_done, 4 * (s - 1) + 2 * b + i + 1)
                    for j in (2 * i, 2 * i + 1):
                        out = p_pre[b][i][:, (j % 2) * HALF:(j % 2 + 1) * HALF]
                        nc.tensor.matmul(out, w1_hi[:, j * P:(j + 1) * P], attr_parts[b][:, :], start=True, stop=False)
                        nc.tensor.matmul(out, w1_lo[:, j * P:(j + 1) * P], attr_parts[b][:, :], start=False, stop=False)
                        for r in range(2):
                            q = 2 * b + r
                            if j == 0:
                                pe.wait_ge(dst_in[q], 16 * (s + 1))
                            last = nc.tensor.matmul(out[:, r * P:(r + 1) * P], rows[q][:, j * P:(j + 1) * P], g.ident[:, :],
                                                    start=False, stop=r == 1, is_transpose=True)
                    last.then_inc(pre_psum, 1)

            def w2(s, b):
                pe.wait_ge(h_lo_ready, 4 * s + 2 * b + 2)
                for i in range(2):
                    if not isinstance(s, int) or 4 * s + 2 * b + i >= 2:
                        pe.wait_ge(m_done, 4 * s + 2 * b + i - 1)
                    nc.tensor.matmul(p_z[i][:, :], ones[:, :], b2_parts[:, :], start=True, stop=False)
                    for j in range(KT):
                        for n, (lhs, rhs) in enumerate(((h_hi[b], w2_hi), (h_hi[b], w2_lo), (h_lo[b], w2_hi))):
                            last = nc.tensor.matmul(p_z[i][:, :], lhs[:, j, i * P:(i + 1) * P], rhs[:, j, :],
                                                    start=False, stop=j == KT - 1 and n == 2)
                    last.then_inc(z_psum, 1)

            def seg(s, b):
                pe.wait_ge(m_done, 4 * s + 2 * b + 2)
                pe.wait_ge(hot_ready, 2 * s + b + 1)
                if b == 0 and (not isinstance(s, int) or s >= 1):
                    pe.wait_ge(agg_done, s)
                for r in range(2):
                    last = nc.tensor.matmul(p_seg[:, :], hot[:, 2 * b + r, :], msg[b][:, r, :],
                                            start=b == 0 and r == 0, stop=b == 1 and r == 1)
                last.then_inc(seg_half, 1)

            state = {}

            def more_tiles():
                more, done = state["window"]
                with pe.If(more > 0):
                    with pe.Fori(0, more) as e:
                        pe.wait_ge(hot_x_ready, done + e + 1)
                        for q in range(SUBS):
                            last = nc.tensor.matmul(p_x[:, :], hot_x[:, q, :], msg[q // 2][:, q % 2, :],
                                                    start=q == 0, stop=q == SUBS - 1)
                        last.then_inc(x_psum, 1)
                pe.nop()

            def step(s, b):
                nxt, prv = after(s, b), before(s, b)
                if b == 0:
                    state["window"] = window(pe, s, both=False)
                if exists(nxt[0]):
                    pre(*nxt)
                w2(s, b)
                if exists(prv[0]):
                    seg(*prv)
                    if b == 0:
                        more_tiles()

            def prologue():
                pe.wait_ge(w_ready, W_READY)
                pre(0, 0)

            def epilogue():
                state["window"] = window(pe, NS, both=False)
                seg(NS - 1, 1)
                more_tiles()

            steps(pe, step, prologue, epilogue)

        @block.scalar
        def _(act):
            def attributes(s, b):
                act.wait_ge(attr_in[b], 32 * (s + 1))
                if not isinstance(s, int) or s >= 1:
                    act.wait_ge(pre_psum, 4 * (s - 1) + 2 * b + 2)
                act.activation(attr_parts[b][:, :], attr[b][:, :], ACT.Copy).then_inc(attr_hi, 1)

            def h(s, b):
                for i in range(2):
                    n = 4 * s + 2 * b + i
                    act.wait_ge(pre_psum, n + 1)
                    if not isinstance(s, int) or s >= 1:
                        act.wait_ge(h_lo_ready, n - 3)
                    act.activation(th[b][i][:, :], p_pre[b][i][:, :], ACT.Exp).then_inc(h_exp, 1)
                for i in range(2):
                    act.wait_ge(h_u, 4 * s + 2 * b + i + 1)
                    act.activation(th[b][i][:, :], th[b][i][:, :], ACT.Ln, bias=1.0, scale=0.5).then_inc(h_ln, 1)
                for i in range(2):
                    act.wait_ge(h_ln, 4 * s + 2 * b + i + 1)
                    act.activation(th[b][i][:, :], th[b][i][:, :], ACT.Exp, scale=-1.0).then_inc(h_inv, 1)
                if not isinstance(s, int) or s >= 1:
                    act.wait_ge(z_psum, 4 * (s - 1) + 2 * b + 2)
                for i in range(2):
                    act.wait_ge(h_done, 4 * s + 2 * b + i + 1)
                    act.activation(h_hi[b][:, 2 * i:2 * i + 2, :], th[b][i][:, :].rearrange("p (j e) -> p j e", j=2), ACT.Copy).then_inc(h_hi_ready, 1)

            def m(s, b):
                for i in range(2):
                    n = 4 * s + 2 * b + i
                    act.wait_ge(z_psum, n + 1)
                    if not isinstance(s, int) or n >= 2:
                        act.wait_ge(m_done, n - 1)
                    act.activation(tz[i][:, :], p_z[i][:, :], ACT.Exp).then_inc(z_exp, 1)
                for i in range(2):
                    act.wait_ge(z_u, 4 * s + 2 * b + i + 1)
                    act.activation(tz[i][:, :], tz[i][:, :], ACT.Ln, bias=1.0, scale=0.5).then_inc(z_ln, 1)
                for i in range(2):
                    act.wait_ge(z_ln, 4 * s + 2 * b + i + 1)
                    act.activation(tz[i][:, :], tz[i][:, :], ACT.Exp, scale=-1.0).then_inc(z_inv, 1)

            def step(s, b):
                nxt, prv = after(s, b), before(s, b)
                if exists(s + 1):
                    attributes(s + 1, b)
                if exists(prv[0]):
                    m(*prv)
                if exists(nxt[0]):
                    h(*nxt)

            def prologue():
                act.wait_ge(w_in, 80)
                act.activation(w2_hi[:, :, :], w2f[:, :, :], ACT.Copy).then_inc(w_ready, 1)
                attributes(0, 0)
                attributes(0, 1)
                h(0, 0)

            steps(act, step, prologue, lambda: m(NS - 1, 1))

        @block.vector
        def _(dve):
            def attributes(s, b):
                dve.wait_ge(attr_hi, 2 * s + b + 1)
                dve.tensor_sub(attr_parts[b][ED:2 * ED, :], attr[b][ED:2 * ED, :],
                               attr_parts[b][ED:2 * ED, :].bitcast(F32)).then_inc(attr_ready, 1)

            def u_of(s, b, t, exp_done, min_done, u_done):
                for i in range(2):
                    dve.wait_ge(exp_done, 4 * s + 2 * b + i + 1)
                    dve.tensor_scalar(t[i][:, :], t[i][:, :], T_MAX, None, ALU.min).then_inc(min_done, 1)
                for i in range(2):
                    dve.wait_ge(min_done, 4 * s + 2 * b + i + 1)
                    dve.scalar_tensor_tensor(out=t[i][:, :], in0=t[i][:, :], scalar=2.0, in1=t[i][:, :],
                                             op0=ALU.add, op1=ALU.mult).then_inc(u_done, 1)

            def h(s, b):
                u_of(s, b, th[b], h_exp, h_min, h_u)
                for i in range(2):
                    dve.wait_ge(h_inv, 4 * s + 2 * b + i + 1)
                    dve.scalar_tensor_tensor(out=th[b][i][:, :], in0=th[b][i][:, :], scalar=1.0, in1=p_pre[b][i][:, :],
                                             op0=ALU.subtract, reverse0=True, op1=ALU.mult).then_inc(h_done, 1)
                for i in range(2):
                    dve.wait_ge(h_hi_ready, 4 * s + 2 * b + i + 1)
                    dve.tensor_sub(h_lo[b][:, 2 * i:2 * i + 2, :], th[b][i][:, :].rearrange("p (j e) -> p j e", j=2),
                                   h_hi[b][:, 2 * i:2 * i + 2, :].bitcast(F32)).then_inc(h_lo_ready, 1)

            def m(s, b):
                u_of(s, b, tz, z_exp, z_min, z_u)
                if not isinstance(s, int) or s >= 1:
                    dve.wait_ge(seg_half, 2 * (s - 1) + b + 1)
                for i in range(2):
                    dve.wait_ge(z_inv, 4 * s + 2 * b + i + 1)
                    dve.scalar_tensor_tensor(out=msg[b][:, i, :], in0=tz[i][:, :], scalar=1.0, in1=p_z[i][:, :],
                                             op0=ALU.subtract, reverse0=True, op1=ALU.mult).then_inc(m_done, 1)

            def one_hot(out, s, q, tile):
                return dve.tensor_scalar(out[:, q, :], g.iota[:, bass.ds(tile * P, P)], g.dstf[:, bass.ds(s * SUBS + q, 1)],
                                         None, ALU.is_equal)

            def add(s, first_tile, more, done):
                dve.wait_ge(seg_half, 2 * s + 2)
                if not isinstance(s, int) or s >= 1:
                    dve.wait_ge(agg_done, s)
                dve.wait_ge(x_added, done + 1)
                dve.tensor_tensor(row(g.agg, first_tile), row(g.agg, first_tile), p_seg[:, :], ALU.add).then_inc(agg_done, 1)
                with dve.If(more > 0):
                    with dve.Fori(0, more) as e:
                        tile = nc.s_assert_le(first_tile + e + 1, NT - 1)
                        for q in range(SUBS):
                            last = one_hot(hot_x, s, q, tile)
                        last.then_inc(hot_x_ready, 1)
                        dve.wait_ge(x_psum, done + e + 1)
                        dve.tensor_tensor(row(g.agg, tile), row(g.agg, tile), p_x[:, :], ALU.add).then_inc(x_added, 1)
                dve.nop()

            def step(s, b):
                nxt, prv = after(s, b), before(s, b)
                if b == 0:
                    state["window"] = window(dve, s)
                tile, tile_before, more, done = state["window"]
                if exists(s + 1):
                    attributes(s + 1, b)
                if exists(prv[0]):
                    m(*prv)
                if exists(nxt[0]):
                    h(*nxt)
                if not isinstance(s, int) or s >= 1:
                    dve.wait_ge(seg_half, 2 * (s - 1) + b + 1)
                for q in (2 * b, 2 * b + 1):
                    last = one_hot(hot, s, q, tile)
                last.then_inc(hot_ready, 1)
                if b == 0 and exists(s - 1):
                    add(s - 1, tile_before, more, done)

            state = {}

            def prologue():
                dve.wait_ge(w_in, 80)
                dve.wait_ge(const_ready, 3)
                dve.tensor_copy(w1_hi[:, :], w1f[:, :]).then_inc(w_ready, 1)
                dve.tensor_copy(ones[:, :], onesf[:, :]).then_inc(w_ready, 1)
                dve.tensor_copy(b2_parts[0:1, :], b2f[0:1, :]).then_inc(w_ready, 1)
                dve.tensor_copy(b2_parts[32:33, :], b2f[32:33, :]).then_inc(w_ready, 1)
                dve.wait_ge(w_ready, 5)
                dve.tensor_sub(w1_lo[:, :], w1f[:, :], w1_hi[:, :].bitcast(F32)).then_inc(w_ready, 1)
                dve.tensor_sub(b2_parts[32:33, :], b2f[32:33, :], b2_parts[32:33, :].bitcast(F32)).then_inc(w_ready, 1)
                dve.tensor_sub(w2_lo[:, :, :], w2f[:, :, :], w2_hi[:, :, :].bitcast(F32)).then_inc(w_ready, 1)
                attributes(0, 0)
                attributes(0, 1)
                h(0, 0)

            def epilogue():
                m(NS - 1, 1)
                _, tile, more, done = window(dve, NS)
                add(NS - 1, tile, more, done)

            steps(dve, step, prologue, epilogue)


W_READY = 8


def update_stage(nc, ctx, g, stage):
    sb = lambda name, shape, dt=F32: stage.enter_context(nc.sbuf_tensor("upd_" + name, shape, dt))
    pb = lambda name, shape: stage.enter_context(nc.psum_tensor("upd_" + name, shape, F32))
    sem = lambda name: stage.enter_context(nc.semaphore("upd_" + name))

    w3, w4 = sb("w3", [P, KT, H]), sb("w4", [P, KT, H])
    b4, gamma, beta = sb("b4", [P, H]), sb("gamma", [P, H]), sb("beta", [P, H])
    two = range(2)
    ag = [sb(f"ag{u}", [P, H]) for u in two]
    aT = [sb(f"aT{u}", [P, KT, P]) for u in two]
    z = [sb(f"z{u}", [P, H]) for u in two]
    tt = [sb(f"tt{u}", [P, H]) for u in two]
    uT = [sb(f"uT{u}", [P, KT, P]) for u in two]
    y = [sb(f"y{u}", [P, H]) for u in two]
    res = [sb(f"res{u}", [P, H]) for u in two]
    stats, mv = [sb(f"stats{u}", [P, 6]) for u in two], [sb(f"mv{u}", [P, 2]) for u in two]
    rstd, shift = [sb(f"rstd{u}", [P, 1]) for u in two], [sb(f"shift{u}", [P, 1]) for u in two]
    p_aT = [pb(f"p_aT{u}", [P, KT * P]) for u in two]
    p_z = [pb(f"p_z{u}", [P, H]) for u in two]
    p_uT = [pb(f"p_uT{u}", [P, KT * P]) for u in two]
    p_y = [pb(f"p_y{u}", [P, H]) for u in two]

    names = """w_in ag_ready aT_psum aT_ready z_psum z_ready t_exp t_min t_u t_ln t_inv u_ready uT_psum uT_ready y_psum
               h1_b4 x1_beta y_half stat_step ln_step shift_ready norm_ready scaled res_ready"""
    (w_in, ag_ready, aT_psum, aT_ready, z_psum, z_ready, t_exp, t_min, t_u, t_ln, t_inv, u_ready, uT_psum, uT_ready, y_psum,
     h1_b4, x1_beta, y_half, stat_step, ln_step, shift_ready, norm_ready, scaled, res_ready) = map(sem, names.split())
    waited = sem("waited")
    stored = [sem(f"stored{u}") for u in two]

    def later(t, n):
        return not isinstance(t, int) or t >= n

    def tiles(eng, body):
        for t in range(2):
            body(t, t)
        with eng.Fori(1, NT // 2) as pair:
            for u in two:
                body(2 * pair + u, u)
        body(NT, 0)

    def into(t):
        return not isinstance(t, int) or t < NT, not isinstance(t, int) or t >= 1

    with nc.Block() as block:

        @block.sync
        def _(sp):
            sp.dma_start(w3[:, :, :], g.w3[H:2 * H, :].rearrange("(k p) n -> p k n", p=P)).then_inc(w_in, 16)
            sp.dma_start(w4[:, :, :], g.w4.rearrange("(k p) n -> p k n", p=P)).then_inc(w_in, 16)
            for to, vector in ((b4, g.b4), (gamma, g.gamma), (beta, g.beta_ln)):
                sp.dma_start(to[:, :], vector.rearrange("(a n) -> a n", a=1).to_broadcast([P, H])).then_inc(w_in, 16)

            def store(t, u, rows=P):
                sp.wait_ge(res_ready, t + 1)
                sp.dma_start(g.out[bass.ds(t * P, rows), :], res[u][0:rows, :]).then_inc(stored[u], 16)

            with sp.Fori(0, NT // 2 - 1) as pair:
                for u in two:
                    store(2 * pair + u, u)
            store(NT - 2, 0)
            store(NT - 1, 1, NODES - (NT - 1) * P)
            for u in two:
                sp.wait_ge(stored[u], 16 * (NT // 2))

        @block.gpsimd
        def _(pool):
            pool.wait_ge(w_in, 80)
            with pool.Fori(0, NT) as t:
                pool.tensor_tensor(row(g.h1, t), row(g.h1, t), b4[:, :], ALU.add).then_inc(h1_b4, 1)
                pool.tensor_tensor(row(g.x1, t), row(g.x1, t), beta[:, :], ALU.add).then_inc(x1_beta, 1)

        @block.tensor
        def _(pe):
            pe.wait_ge(w_in, 80)

            def body(t, u):
                new, old = into(t)
                if new:
                    pe.wait_ge(ag_ready, t + 1)
                    if later(t, 2):
                        pe.wait_ge(aT_ready, t - 1)
                    for k in range(KT):
                        last = nc.tensor.transpose(p_aT[u][:, k * P:(k + 1) * P], ag[u][:, k * P:(k + 1) * P], g.ident[:, :])
                    last.then_inc(aT_psum, 1)
                if old:
                    v = 1 - u
                    pe.wait_ge(u_ready, t)
                    if later(t, 3):
                        pe.wait_ge(uT_ready, t - 2)
                    for k in range(KT):
                        last = nc.tensor.transpose(p_uT[v][:, k * P:(k + 1) * P], z[v][:, k * P:(k + 1) * P], g.ident[:, :])
                    last.then_inc(uT_psum, 1)
                if new:
                    pe.wait_ge(aT_ready, t + 1)
                    if later(t, 2):
                        pe.wait_ge(z_ready, t - 1)
                    for k in range(KT):
                        last = nc.tensor.matmul(p_z[u][:, :], aT[u][:, k, :], w3[:, k, :], start=k == 0, stop=k == KT - 1)
                    last.then_inc(z_psum, 1)
                if old:
                    pe.wait_ge(uT_ready, t)
                    if later(t, 3):
                        pe.wait_ge(y_half, t - 2)
                    for k in range(KT):
                        last = nc.tensor.matmul(p_y[v][:, :], uT[v][:, k, :], w4[:, k, :], start=k == 0, stop=k == KT - 1)
                    last.then_inc(y_psum, 1)

            tiles(pe, body)

        @block.scalar
        def _(act):
            def take(t, u):
                if later(t, 2):
                    act.wait_ge(aT_psum, t - 1)
                act.activation(ag[u][:, :], row(g.agg, t), ACT.Copy).then_inc(ag_ready, 1)

            def body(t, u):
                new, old = into(t)
                if new:
                    take(t, u)
                if old:
                    v = 1 - u
                    act.wait_ge(uT_psum, t)
                    if later(t, 3):
                        act.wait_ge(y_psum, t - 2)
                    act.activation(uT[v][:, :, :], p_uT[v][:, :].rearrange("p (k m) -> p k m", k=KT), ACT.Copy).then_inc(uT_ready, 1)
                if new:
                    act.wait_ge(t_min, t + 1)
                    act.activation(tt[u][:, :], tt[u][:, :], ACT.Exp).then_inc(t_exp, 1)
                    act.wait_ge(t_u, t + 1)
                    act.activation(tt[u][:, :], tt[u][:, :], ACT.Ln, bias=1.0, scale=0.5).then_inc(t_ln, 1)
                    act.wait_ge(t_ln, t + 1)
                    act.activation(tt[u][:, :], tt[u][:, :], ACT.Exp, scale=-1.0).then_inc(t_inv, 1)
                if old:
                    act.wait_ge(stat_step, 2 * t)
                    if later(t, 3):
                        act.wait_ge(norm_ready, t - 2)
                    act.activation(rstd[v][:, :], mv[v][:, 1:2], ACT.Ln, bias=g.eps[:, 0:1]).then_inc(ln_step, 1)
                    act.wait_ge(ln_step, 2 * t - 1)
                    act.activation(rstd[v][:, :], rstd[v][:, :], ACT.Exp, scale=-0.5).then_inc(ln_step, 1)
                    act.wait_ge(shift_ready, t)
                    act.activation(y[v][:, :], y[v][:, :], ACT.Identity, bias=shift[v][:, 0:1], scale=rstd[v][:, 0:1]).then_inc(norm_ready, 1)

            tiles(act, body)

        @block.vector
        def _(dve):
            dve.wait_ge(w_in, 80)
            def body(t, u):
                new, old = into(t)
                if new:
                    dve.wait_ge(aT_psum, t + 1)
                    if later(t, 2):
                        dve.wait_ge(z_psum, t - 1)
                    dve.tensor_copy(aT[u][:, :, :], p_aT[u][:, :].rearrange("p (k m) -> p k m", k=KT)).then_inc(aT_ready, 1)
                    dve.wait_ge(z_psum, t + 1)
                    if later(t, 2):
                        dve.wait_ge(uT_psum, t - 1)
                    dve.tensor_tensor(z[u][:, :], p_z[u][:, :], row(g.own, t), ALU.add).then_inc(z_ready, 1)
                    dve.wait_ge(z_ready, t + 1)
                    if later(t, 2):
                        dve.wait_ge(u_ready, t - 1)
                    dve.tensor_scalar(tt[u][:, :], z[u][:, :], X_MAX, None, ALU.min).then_inc(t_min, 1)
                    dve.wait_ge(t_exp, t + 1)
                    dve.scalar_tensor_tensor(out=tt[u][:, :], in0=tt[u][:, :], scalar=2.0, in1=tt[u][:, :],
                                             op0=ALU.add, op1=ALU.mult).then_inc(t_u, 1)
                    dve.wait_ge(t_inv, t + 1)
                    dve.scalar_tensor_tensor(out=z[u][:, :], in0=tt[u][:, :], scalar=1.0, in1=z[u][:, :],
                                             op0=ALU.subtract, reverse0=True, op1=ALU.mult).then_inc(u_ready, 1)
                if old:
                    v = 1 - u
                    one = slice(None), bass.ds(t - 1, 1)
                    dve.wait_ge(y_psum, t)
                    dve.wait_ge(h1_b4, t)
                    if later(t, 3):
                        dve.wait_ge(scaled, t - 2)
                    dve.tensor_tensor(y[v][:, :], p_y[v][:, :], row(g.h1, t - 1), ALU.add).then_inc(y_half, 1)
                    dve.wait_ge(y_half, t)
                    dve.bn_stats(stats[v][:, :], y[v][:, :]).then_inc(stat_step, 1)
                    dve.wait_ge(stat_step, 2 * t - 1)
                    dve.sem_inc(waited, 1)
                    dve.bn_aggr(mv[v][:, :], stats[v][:, :]).then_inc(stat_step, 1)
                    dve.wait_ge(ln_step, 2 * t)
                    dve.scalar_tensor_tensor(out=shift[v][:, :], in0=mv[v][:, 0:1], scalar=-1.0, in1=rstd[v][:, :],
                                             op0=ALU.mult, op1=ALU.mult).then_inc(shift_ready, 1)
                    dve.wait_ge(norm_ready, t)
                    if later(t, 3):
                        dve.wait_ge(stored[v], 8 * (t - 1 - v))
                    dve.scalar_tensor_tensor(out=res[v][:, :], in0=y[v][:, :], scalar=g.nan0[one], in1=gamma[:, :],
                                             op0=ALU.add, op1=ALU.mult).then_inc(scaled, 1)
                    dve.wait_ge(scaled, t)
                    dve.wait_ge(x1_beta, t)
                    dve.tensor_tensor(res[v][:, :], res[v][:, :], row(g.x1, t - 1), ALU.add).then_inc(res_ready, 1)

            tiles(dve, body)


def gnn_kernel(nc, x, src_cols, dst_cols, dst_rows, attr_t, wc, wn, bias, w1, b1, w2, b2, w3, b3, w4, b4, gamma, beta_ln, out):
    g = Net()
    g.x, g.src_cols, g.dst_cols, g.dst_rows, g.attr_t, g.out = x, src_cols, dst_cols, dst_rows, attr_t, out
    g.wc, g.wn, g.bias, g.w1, g.b1, g.w2, g.b2, g.w3, g.b3, g.w4, g.b4 = wc, wn, bias, w1, b1, w2, b2, w3, b3, w4, b4
    g.gamma, g.beta_ln = gamma, beta_ln
    g.spans = nc.dram_tensor("spans", [NT, 4], I32, kind="Internal").ap()
    g.wins = nc.dram_tensor("wins", [NS + 1, 4], I32, kind="Internal").ap()
    g.tab_src = nc.dram_tensor("tab_src", [NP, H], F32, kind="Internal").ap()
    g.tab_dst = nc.dram_tensor("tab_dst", [NP, H], F32, kind="Internal").ap()
    with ExitStack() as ctx:
        sb = lambda name, shape, dt=F32: ctx.enter_context(nc.sbuf_tensor("net_" + name, shape, dt))
        g.x1 = sb("x1", [P, NT, H])
        g.ident = sb("ident", [P, P])
        g.iota, g.iota16 = sb("iota", [P, NP]), sb("iota16", [P, NP], F16)
        g.src_i, g.dst_i = sb("src_i", [P, NSUB], I32), sb("dst_i", [P, NSUB], I32)
        g.srcf, g.dstf = sb("srcf", [P, NSUB]), sb("dstf", [P, NSUB])
        g.nan0, g.eps = sb("nan0", [P, NT]), sb("eps", [P, 1])
        g.own, g.h1 = sb("own", [P, NT, H]), sb("h1", [P, NT, H])
        with ExitStack() as first:
            g.beta = first.enter_context(nc.sbuf_tensor("net_beta", [P, NT, H], F32))
            g.adj = first.enter_context(nc.sbuf_tensor("net_adj", [P, NT, NP], F32))
            with ExitStack() as stage:
                prepare_stage(nc, ctx, g, stage)
            with ExitStack() as stage:
                adjacency_stage(nc, ctx, g, stage)
            with ExitStack() as stage:
                node_stage(nc, ctx, g, stage)
        g.agg = sb("agg", [P, NT, H])
        with ExitStack() as stage:
            edge_stage(nc, ctx, g, stage)
        with ExitStack() as stage:
            update_stage(nc, ctx, g, stage)


def kernel(x, src, dst, edge_attr_64, L0_gnn_wc, L0_gnn_wn, L0_gnn_bias, L1_gnn_W1, L1_gnn_b1, L1_gnn_W2, L1_gnn_b2,
           L1_gnn_W3, L1_gnn_b3, L1_gnn_W4, L1_gnn_b4, L1_gnn_gamma, L1_gnn_beta):
    import numpy as np
    import concourse.bacc as bacc
    from concourse.bass_utils import run_bass_kernel_spmd

    more = NS * SUPER - EDGES
    src = np.pad(np.asarray(src), (0, more), constant_values=PAD_NODE)
    dst = np.pad(np.asarray(dst), (0, more), constant_values=PAD_NODE)
    arrays = {
        "x": np.pad(np.asarray(x), ((0, NP - NODES), (0, 0))),
        "src_cols": src.reshape(NSUB, P).T,
        "dst_cols": dst.reshape(NSUB, P).T,
        "dst_rows": dst.reshape(NS, SUPER),
        "attr_t": np.pad(np.asarray(edge_attr_64), ((0, more), (0, 0))).T,
        "wc": L0_gnn_wc, "wn": L0_gnn_wn, "bias": L0_gnn_bias, "w1": L1_gnn_W1, "b1": L1_gnn_b1, "w2": L1_gnn_W2,
        "b2": L1_gnn_b2, "w3": L1_gnn_W3, "b3": L1_gnn_b3, "w4": L1_gnn_W4, "b4": L1_gnn_b4, "gamma": L1_gnn_gamma,
        "beta_ln": L1_gnn_beta,
    }
    nc = bacc.Bacc("TRN2", target_bir_lowering=False, num_devices=1)
    feeds, args = {}, []
    for name, array in arrays.items():
        array = np.ascontiguousarray(array)
        feeds["in_" + name] = array
        args.append(nc.dram_tensor("in_" + name, array.shape, mybir.dt.from_np(array.dtype), kind="ExternalInput").ap())
    out = nc.dram_tensor("out_x", [NODES, H], F32, kind="ExternalOutput").ap()
    gnn_kernel(nc, *args, out)
    r = run_bass_kernel_spmd(nc, [feeds], core_ids=[0])
    return r.results[0]["out_x"]
```
